# Optimizing a Trainium2 kernel written in Bass

```python
import numpy as np
import jax
import jax.numpy as jnp

def _softmax(x, axis=-1):
    return jax.nn.softmax(x, axis=axis)

def _gelu(x):
    return jax.nn.gelu(x, approximate=True)

def _silu(x):
    return jax.nn.silu(x)

def _sigmoid(x):
    return jax.nn.sigmoid(x)

def _layernorm(x, axis=-1, eps=1e-05):
    m = jnp.mean(x, axis=axis, keepdims=True)
    v = jnp.var(x, axis=axis, keepdims=True)
    return (x - m) / jnp.sqrt(v + eps)

def _scatter_add(tgt, idx, src, axis=0):
    return tgt.at[idx].add(src)

def _segment_sum(src, seg, n):
    return jax.ops.segment_sum(src, seg, n)
kernel_name = 'mk_dlrm_tower_d1_rec_r8_a25f33'

def setup_inputs(seed: int=0):
    np.random.seed(seed)
    _w = jnp.asarray

    def _rec_inputs():
        import jax
        import jax.numpy as jnp
        _tk = jax.random.key(seed)
        dense_ctx = jax.random.normal(jax.random.fold_in(_tk, 190), (512, 16), jnp.float32)
        ids = jnp.stack([jax.random.randint(jax.random.fold_in(_tk, 200 + f), (512,), 0, v, jnp.int32) for f, v in enumerate([125000, 125000, 125000, 1250, 1000, 12500, 12500, 12500, 1250, 1250, 1000, 1250, 1250, 1000, 1250, 1250, 1000, 1250, 1250, 1000, 1250, 1250, 1250, 1250, 1250, 12500, 1250, 12500, 12500, 1250, 12500, 1250])], axis=1)
        tbl_0 = 0.05 * jax.random.normal(jax.random.fold_in(_tk, 500 + 0), (125000, 64), jnp.float32)
        tbl_1 = 0.05 * jax.random.normal(jax.random.fold_in(_tk, 500 + 1), (125000, 64), jnp.float32)
        tbl_2 = 0.05 * jax.random.normal(jax.random.fold_in(_tk, 500 + 2), (125000, 64), jnp.float32)
        tbl_3 = 0.05 * jax.random.normal(jax.random.fold_in(_tk, 500 + 3), (1250, 64), jnp.float32)
        tbl_4 = 0.05 * jax.random.normal(jax.random.fold_in(_tk, 500 + 4), (1000, 64), jnp.float32)
        tbl_5 = 0.05 * jax.random.normal(jax.random.fold_in(_tk, 500 + 5), (12500, 64), jnp.float32)
        tbl_6 = 0.05 * jax.random.normal(jax.random.fold_in(_tk, 500 + 6), (12500, 64), jnp.float32)
        tbl_7 = 0.05 * jax.random.normal(jax.random.fold_in(_tk, 500 + 7), (12500, 64), jnp.float32)
        tbl_8 = 0.05 * jax.random.normal(jax.random.fold_in(_tk, 500 + 8), (1250, 64), jnp.float32)
        tbl_9 = 0.05 * jax.random.normal(jax.random.fold_in(_tk, 500 + 9), (1250, 64), jnp.float32)
        tbl_10 = 0.05 * jax.random.normal(jax.random.fold_in(_tk, 500 + 10), (1000, 64), jnp.float32)
        tbl_11 = 0.05 * jax.random.normal(jax.random.fold_in(_tk, 500 + 11), (1250, 64), jnp.float32)
        tbl_12 = 0.05 * jax.random.normal(jax.random.fold_in(_tk, 500 + 12), (1250, 64), jnp.float32)
        tbl_13 = 0.05 * jax.random.normal(jax.random.fold_in(_tk, 500 + 13), (1000, 64), jnp.float32)
        tbl_14 = 0.05 * jax.random.normal(jax.random.fold_in(_tk, 500 + 14), (1250, 64), jnp.float32)
        tbl_15 = 0.05 * jax.random.normal(jax.random.fold_in(_tk, 500 + 15), (1250, 64), jnp.float32)
        tbl_16 = 0.05 * jax.random.normal(jax.random.fold_in(_tk, 500 + 16), (1000, 64), jnp.float32)
        tbl_17 = 0.05 * jax.random.normal(jax.random.fold_in(_tk, 500 + 17), (1250, 64), jnp.float32)
        tbl_18 = 0.05 * jax.random.normal(jax.random.fold_in(_tk, 500 + 18), (1250, 64), jnp.float32)
        tbl_19 = 0.05 * jax.random.normal(jax.random.fold_in(_tk, 500 + 19), (1000, 64), jnp.float32)
        tbl_20 = 0.05 * jax.random.normal(jax.random.fold_in(_tk, 500 + 20), (1250, 64), jnp.float32)
        tbl_21 = 0.05 * jax.random.normal(jax.random.fold_in(_tk, 500 + 21), (1250, 64), jnp.float32)
        tbl_22 = 0.05 * jax.random.normal(jax.random.fold_in(_tk, 500 + 22), (1250, 64), jnp.float32)
        tbl_23 = 0.05 * jax.random.normal(jax.random.fold_in(_tk, 500 + 23), (1250, 64), jnp.float32)
        tbl_24 = 0.05 * jax.random.normal(jax.random.fold_in(_tk, 500 + 24), (1250, 64), jnp.float32)
        tbl_25 = 0.05 * jax.random.normal(jax.random.fold_in(_tk, 500 + 25), (12500, 64), jnp.float32)
        tbl_26 = 0.05 * jax.random.normal(jax.random.fold_in(_tk, 500 + 26), (1250, 64), jnp.float32)
        tbl_27 = 0.05 * jax.random.normal(jax.random.fold_in(_tk, 500 + 27), (12500, 64), jnp.float32)
        tbl_28 = 0.05 * jax.random.normal(jax.random.fold_in(_tk, 500 + 28), (12500, 64), jnp.float32)
        tbl_29 = 0.05 * jax.random.normal(jax.random.fold_in(_tk, 500 + 29), (1250, 64), jnp.float32)
        tbl_30 = 0.05 * jax.random.normal(jax.random.fold_in(_tk, 500 + 30), (12500, 64), jnp.float32)
        tbl_31 = 0.05 * jax.random.normal(jax.random.fold_in(_tk, 500 + 31), (1250, 64), jnp.float32)
        _rk = jax.random.fold_in(_tk, 7)
        W_top1 = 0.0606339 * jax.random.normal(jax.random.fold_in(_tk, 801), (272, 512), jnp.float32)
        W_top2 = 0.0441942 * jax.random.normal(jax.random.fold_in(_tk, 802), (512, 256), jnp.float32)
        W_top3 = 0.0625 * jax.random.normal(jax.random.fold_in(_tk, 803), (256, 1), jnp.float32)
        b_top1 = jnp.zeros((512,), jnp.float32)
        b_top2 = jnp.zeros((256,), jnp.float32)
        return (dense_ctx, ids, tbl_0, tbl_1, tbl_2, tbl_3, tbl_4, tbl_5, tbl_6, tbl_7, tbl_8, tbl_9, tbl_10, tbl_11, tbl_12, tbl_13, tbl_14, tbl_15, tbl_16, tbl_17, tbl_18, tbl_19, tbl_20, tbl_21, tbl_22, tbl_23, tbl_24, tbl_25, tbl_26, tbl_27, tbl_28, tbl_29, tbl_30, tbl_31, W_top1, b_top1, W_top2, b_top2, W_top3)
    dense_ctx, ids, tbl_0, tbl_1, tbl_2, tbl_3, tbl_4, tbl_5, tbl_6, tbl_7, tbl_8, tbl_9, tbl_10, tbl_11, tbl_12, tbl_13, tbl_14, tbl_15, tbl_16, tbl_17, tbl_18, tbl_19, tbl_20, tbl_21, tbl_22, tbl_23, tbl_24, tbl_25, tbl_26, tbl_27, tbl_28, tbl_29, tbl_30, tbl_31, W_top1, b_top1, W_top2, b_top2, W_top3 = _rec_inputs()

    def _L0_rec_setup():
        import jax, jax.numpy as jnp
        import numpy as np
        NUM_COLS = 32
        EMBED_DIM = 64
        LAYER_DIMS = [128, 128]
        BATCH = 1024

        def _cin_layer(X, prev_x, W, b):
            bsz, m, d = X.shape
            h = prev_x.shape[1]
            x_i = jnp.einsum('bmd,bhd->bmhd', X, prev_x).reshape(bsz, m * h, d)
            x_i = jnp.einsum('oc,bcd->bod', W, x_i) + b[None, :, None]
            return x_i
        key = jax.random.key(seed)
        k_x, k_w0, k_w1 = jax.random.split(key, 3)
        X = jax.random.normal(k_x, (BATCH, NUM_COLS, EMBED_DIM), dtype=jnp.float32)
        in0 = NUM_COLS * NUM_COLS
        in1 = NUM_COLS * LAYER_DIMS[0]
        W0 = jax.random.normal(k_w0, (LAYER_DIMS[0], in0), dtype=jnp.float32) * (1.0 / np.sqrt(in0))
        b0 = jnp.zeros((LAYER_DIMS[0],), dtype=jnp.float32)
        W1 = jax.random.normal(k_w1, (LAYER_DIMS[1], in1), dtype=jnp.float32) * (1.0 / np.sqrt(in1))
        b1 = jnp.zeros((LAYER_DIMS[1],), dtype=jnp.float32)
        return {'X': X, 'W0': W0, 'b0': b0, 'W1': W1, 'b1': b1}
    _L0_rec_all = _L0_rec_setup()
    _L0_rec_in = {k: v for k, v in _L0_rec_all.items() if k in ('W0', 'b0', 'W1', 'b1')}
    del _L0_rec_all
    return {'dense_ctx': dense_ctx, 'ids': ids, 'tbl_0': tbl_0, 'tbl_1': tbl_1, 'tbl_2': tbl_2, 'tbl_3': tbl_3, 'tbl_4': tbl_4, 'tbl_5': tbl_5, 'tbl_6': tbl_6, 'tbl_7': tbl_7, 'tbl_8': tbl_8, 'tbl_9': tbl_9, 'tbl_10': tbl_10, 'tbl_11': tbl_11, 'tbl_12': tbl_12, 'tbl_13': tbl_13, 'tbl_14': tbl_14, 'tbl_15': tbl_15, 'tbl_16': tbl_16, 'tbl_17': tbl_17, 'tbl_18': tbl_18, 'tbl_19': tbl_19, 'tbl_20': tbl_20, 'tbl_21': tbl_21, 'tbl_22': tbl_22, 'tbl_23': tbl_23, 'tbl_24': tbl_24, 'tbl_25': tbl_25, 'tbl_26': tbl_26, 'tbl_27': tbl_27, 'tbl_28': tbl_28, 'tbl_29': tbl_29, 'tbl_30': tbl_30, 'tbl_31': tbl_31, 'W_top1': W_top1, 'b_top1': b_top1, 'W_top2': W_top2, 'b_top2': b_top2, 'W_top3': W_top3, 'L0_rec_W0': _L0_rec_in['W0'], 'L0_rec_b0': _L0_rec_in['b0'], 'L0_rec_W1': _L0_rec_in['W1'], 'L0_rec_b1': _L0_rec_in['b1']}

def reference(dense_ctx, ids, tbl_0, tbl_1, tbl_2, tbl_3, tbl_4, tbl_5, tbl_6, tbl_7, tbl_8, tbl_9, tbl_10, tbl_11, tbl_12, tbl_13, tbl_14, tbl_15, tbl_16, tbl_17, tbl_18, tbl_19, tbl_20, tbl_21, tbl_22, tbl_23, tbl_24, tbl_25, tbl_26, tbl_27, tbl_28, tbl_29, tbl_30, tbl_31, W_top1, b_top1, W_top2, b_top2, W_top3, L0_rec_W0, L0_rec_b0, L0_rec_W1, L0_rec_b1):
    import jax
    import jax.numpy as jnp

    def _L0_rec_ref(X, W0, b0, W1, b1):
        import jax, jax.numpy as jnp
        import numpy as np
        NUM_COLS = 32
        EMBED_DIM = 64
        LAYER_DIMS = [128, 128]
        BATCH = 1024

        def _cin_layer(X, prev_x, W, b):
            bsz, m, d = X.shape
            h = prev_x.shape[1]
            x_i = jnp.einsum('bmd,bhd->bmhd', X, prev_x).reshape(bsz, m * h, d)
            x_i = jnp.einsum('oc,bcd->bod', W, x_i) + b[None, :, None]
            return x_i
        prev_x = X
        cin_outs = []
        for W, b in ((W0, b0), (W1, b1)):
            x_i = _cin_layer(X, prev_x, W, b)
            cin_outs.append(x_i.sum(axis=2))
            prev_x = x_i
        return jnp.concatenate(cin_outs, axis=1)
    e = jnp.stack([tbl_0[ids[:, 0]], tbl_1[ids[:, 1]], tbl_2[ids[:, 2]], tbl_3[ids[:, 3]], tbl_4[ids[:, 4]], tbl_5[ids[:, 5]], tbl_6[ids[:, 6]], tbl_7[ids[:, 7]], tbl_8[ids[:, 8]], tbl_9[ids[:, 9]], tbl_10[ids[:, 10]], tbl_11[ids[:, 11]], tbl_12[ids[:, 12]], tbl_13[ids[:, 13]], tbl_14[ids[:, 14]], tbl_15[ids[:, 15]], tbl_16[ids[:, 16]], tbl_17[ids[:, 17]], tbl_18[ids[:, 18]], tbl_19[ids[:, 19]], tbl_20[ids[:, 20]], tbl_21[ids[:, 21]], tbl_22[ids[:, 22]], tbl_23[ids[:, 23]], tbl_24[ids[:, 24]], tbl_25[ids[:, 25]], tbl_26[ids[:, 26]], tbl_27[ids[:, 27]], tbl_28[ids[:, 28]], tbl_29[ids[:, 29]], tbl_30[ids[:, 30]], tbl_31[ids[:, 31]]], axis=1)
    z = _L0_rec_ref(e, L0_rec_W0, L0_rec_b0, L0_rec_W1, L0_rec_b1)
    z = z.reshape(z.shape[0], -1)
    h = jnp.concatenate([z, dense_ctx], axis=1)
    h = jnp.maximum(h @ W_top1 + b_top1, 0.0)
    h = jnp.maximum(h @ W_top2 + b_top2, 0.0)
    y = h @ W_top3
    return y

_drawn_inputs = setup_inputs


def setup_inputs(seed=0):
    import zlib

    import numpy as np

    out = dict(_drawn_inputs(seed))
    spreads = {'b_top1': (0.0, 1.364),
     'b_top2': (0.0, 0.551),
     'L0_rec_b0': (0.0, 0.1),
     'L0_rec_b1': (0.0, 0.1)}
    factors = {'tbl_0': 8.0,
     'tbl_1': 8.0,
     'tbl_2': 8.0,
     'tbl_3': 8.0,
     'tbl_4': 8.0,
     'tbl_5': 8.0,
     'tbl_6': 8.0,
     'tbl_7': 8.0,
     'tbl_8': 8.0,
     'tbl_9': 8.0,
     'tbl_10': 8.0,
     'tbl_11': 8.0,
     'tbl_12': 8.0,
     'tbl_13': 8.0,
     'tbl_14': 8.0,
     'tbl_15': 8.0,
     'tbl_16': 8.0,
     'tbl_17': 8.0,
     'tbl_18': 8.0,
     'tbl_19': 8.0,
     'tbl_20': 8.0,
     'tbl_21': 8.0,
     'tbl_22': 8.0,
     'tbl_23': 8.0,
     'tbl_24': 8.0,
     'tbl_25': 8.0,
     'tbl_26': 8.0,
     'tbl_27': 8.0,
     'tbl_28': 8.0,
     'tbl_29': 8.0,
     'tbl_30': 8.0,
     'tbl_31': 8.0,
     'L0_rec_W0': 8.0,
     'L0_rec_W1': 5.645,
     'dense_ctx': 3.35}
    for name, (base, spread) in spreads.items():
        noise = np.random.default_rng([zlib.crc32(name.encode()), seed]).standard_normal(out[name].shape)
        drawn = base * np.exp(spread * noise) if base else spread * noise
        out[name] = jnp.asarray(drawn.astype(out[name].dtype))
    for name, factor in factors.items():
        out[name] = (out[name] * factor).astype(out[name].dtype)
    return out
```

```python
import concourse.bass as bass
from concourse import mybir
from contextlib import ExitStack
import numpy as np

B = 512
M = 32
D = 64
O = 128
HALF = M // 2
SHIFTS = 4
LAST = 4
PAIRS = SHIFTS * HALF + LAST
GRAM = HALF // 2
COLS = PAIRS + GRAM + 1
VCOLS = PAIRS + 1
UNIT = 32
SUB = UNIT // 2
GROUP = 8
UNITS = 4
CHUNK = UNIT * UNITS
CHUNKS = B // CHUNK
PER_GATHER = 128 // M
TILES = UNIT // PER_GATHER
TOP1, TOP2 = 512, 256
DENSE = 16
BANK = 512
W1_CHUNKS = 4


def build(nc, table, ids, base, w1t, w0p, w0x, w0g, cin_b, top1, top1d, top2, top3, b_top, dense, out):
    F32, I32 = mybir.dt.float32, mybir.dt.int32
    ALU, ACT = mybir.AluOpType, mybir.ActivationFunctionType

    with ExitStack() as ctx:
        def sb(name, cols, dt=F32):
            return ctx.enter_context(nc.sbuf_tensor(name, [128, cols], dt))

        def sem(name):
            return ctx.enter_context(nc.semaphore(name))

        def at(t, col, dims, part=0, parts=128):
            row = t[:, :].ap[0][0]
            return bass.AP(t[:, :].tensor, part * row + col, [[row, parts]] + dims)

        t_sb = sb("t_sb", 2 * COLS * CHUNK)
        coef = sb("coef", VCOLS * O)
        coef_t_at = COLS * CHUNK
        rows = sb("rows", UNITS * TILES * D)
        prod = [sb(f"prod{n}", SUB * 2 * COLS) for n in range(4)]
        xbd = [sb(f"xbd{n}", UNIT * 2 * M) for n in range(2)]
        xx = [sb(f"xx{n}", UNIT * 2 * HALF) for n in range(2)]
        w1_sb = sb("w1_sb", M * O)
        w0p_sb = sb("w0p_sb", 4 * VCOLS)
        w0x_sb = sb("w0x_sb", 2 * 2 * HALF * HALF)
        w0g_sb = w0x_sb
        ident = sb("ident", 128)
        cin_bias = sb("cin_bias", 4)
        top_bias = sb("top_bias", 6)
        top3_sb = sb("top3_sb", 2)
        idx = sb("idx", UNITS * CHUNKS * TILES, I32)

        cross = coef
        pair_in, cross_in, base_in = 0, 2 * 4 * VCOLS, 2 * 4 * VCOLS + 4 * HALF * HALF
        ids_in = base_in + idx.shape[1]
        top1_at, top1d_at = 0, 2 * TOP1
        top2_at = top1d_at + 128
        dense_at = top2_at + 4 * TOP2
        z_at = dense_at + B
        hid1, hid2 = prod[0:2], prod[2]

        psum = ctx.enter_context(nc.psum_tensor("psum", [128, 8 * BANK], F32))

        def bank(n, col=0, cols=BANK, part=0, parts=128):
            return psum[part:part + parts, n * BANK + col:n * BANK + col + cols]

        XT = 0
        SPARE = 1
        TG = 2
        ACC = 6
        L3 = TG + 2
        L1 = XT
        C_BANKS = (ACC, ACC + 1, SPARE, TG)
        W_BANKS = (ACC, ACC + 1, SPARE)

        ids_in_sb = sem("ids_in_sb")
        w0p_in_sb, w0x_in_sb = sem("w0p_in_sb"), sem("w0x_in_sb")
        w1_in_sb = [sem(f"w1_in_sb{n}") for n in range(W1_CHUNKS)]
        small_in_sb = sem("small_in_sb")
        top_in_sb = sem("top_in_sb")
        w0g_in_sb = sem("w0g_in_sb")
        idx_ready = sem("idx_ready")
        ident_zero, ident_ready = sem("ident_zero"), sem("ident_ready")
        gathered = [sem(f"gathered{s}") for s in range(UNITS)]
        xt_done = sem("xt_done")
        xx_ready = sem("xx_ready")
        xbd_ready = sem("xbd_ready")
        prod_ready = sem("prod_ready")
        fills_ready = sem("fills_ready")
        w0_ready = sem("w0_ready")
        bias_ready = sem("bias_ready")
        t_done = sem("t_done")
        t_copied = [sem(f"t_copied{p}") for p in range(2)]
        cin1_done = sem("cin1_done")
        t_free = sem("t_free")
        u_done = sem("u_done")
        u_pairs = sem("u_pairs")
        u_cross = sem("u_cross")
        fold_step = sem("fold_step")
        pool_step = sem("pool_step")
        coef_tr = sem("coef_tr")
        coef_ready = [sem(f"coef_ready{n}") for n in range(2)]
        acc_free = sem("acc_free")
        l1_done, l1_ready = sem("l1_done"), sem("l1_ready")
        l2_done, l2_ready = sem("l2_done"), sem("l2_ready")
        l3_done, l3_ready = sem("l3_done"), sem("l3_ready")
        stored = sem("stored")

        W_PARTS = [(14, 16, 17, 19), (19, 21, 23, 25), (25, 27, 29, 32)]

        TOP_DMAS = 3 + 2 * TOP1 // 128
        V_GROUPS = -(-VCOLS // 4)
        COPIER = [n % 3 // 2 for n in range(V_GROUPS)]
        DVE_SHIFTS, POOL_SHIFTS = range(0, 5), range(5, 8)
        FOLD_AT = 6 * TILES + 2

        def wait(eng, s, n):
            if not isinstance(n, int) or n > 0:
                eng.wait_ge(s, n)

        block = ctx.enter_context(nc.Block())

        @block.sync
        def _(sp):
            sp.dma_start(at(t_sb, ids_in, [[1, idx.shape[1]]]).bitcast(I32), ids).then_inc(ids_in_sb, 16)
            sp.dma_start(at(t_sb, base_in, [[1, idx.shape[1]]]).bitcast(I32), base).then_inc(ids_in_sb, 16)
            for n in range(W1_CHUNKS):
                w = M * O // W1_CHUNKS
                sp.dma_start(w1_sb[:, n * w:(n + 1) * w], w1t[:, n * w:(n + 1) * w]).then_inc(w1_in_sb[n], 16)
            sp.dma_start(cin_bias[:, 0:2], cin_b).then_inc(small_in_sb, 16)
            sp.dma_start(top_bias[:, :], b_top).then_inc(small_in_sb, 16)
            sp.wait_ge(u_done, 2 * M)
            sp.dma_start(w0g_sb[:, :], w0g).then_inc(w0g_in_sb, 16)
            sp.dma_start(w1_sb[:, top1_at:top1_at + 2 * TOP1], top1).then_inc(top_in_sb, 16)
            sp.dma_start(w1_sb[:, top2_at:top2_at + 4 * TOP2], top2).then_inc(top_in_sb, 16)
            sp.dma_start(top3_sb[:, :], top3).then_inc(top_in_sb, 16)
            for j in range(TOP1 // 128):
                sp.dma_start(w1_sb[32 * j:32 * j + DENSE, top1d_at:top1d_at + 128], top1d[:, 128 * j:128 * (j + 1)])\
                    .then_inc(top_in_sb, 16)
                sp.dma_start(w1_sb[32 * j:32 * j + DENSE, dense_at:dense_at + B], dense).then_inc(top_in_sb, 16)
            sp.wait_ge(l3_ready, 2)
            row = prod[3][:, :].ap[0][0]
            sp.dma_start(out, bass.AP(prod[3][:, :].tensor, 0, [[32 * row, 4], [1, B // 4]])).then_inc(stored, 16)
            sp.wait_ge(stored, 16)


        def transpose_rows(pe, q, s):
            u = UNITS * q + s
            pe.wait_ge(gathered[s], (q + 1) * 16 * TILES)
            wait(pe, xx_ready, 2 * u)
            wait(pe, xbd_ready, 2 * u)
            for t in range(TILES // 2):
                c = (s * TILES + 2 * t) * D
                last = pe.matmul(bank(XT, 128 * t, 128), rows[:, c:c + 2 * D], ident[:, :],
                                 is_transpose=True, start=True, stop=True)
            last.then_inc(xt_done, 1)

        def copy_xx(act, q, s, g):
            for k in range(2):
                src = at(psum, XT * BANK + HALF * k, [[M, SUB], [0, 2], [1, HALF]], D * g, D)
                dst = at(xx[s % 2], g * SUB * 2 * HALF, [[2 * HALF, SUB], [HALF, 2], [1, HALF]], D * k, D)
                last = act.activation(dst, src, ACT.Copy)
            last.then_inc(xx_ready, 1)

        def copy_xbd(act, q, s, g):
            for k in range(2):
                src = at(psum, XT * BANK, [[M, SUB], [1, M]], D * g, D)
                dst = at(xbd[s % 2], g * SUB * 2 * M + M * k, [[2 * M, SUB], [1, M]], D * k, D)
                last = act.activation(dst, src, ACT.Copy)
            last.then_inc(xbd_ready, 1)

        def t_group(pe, q, s, v):
            u = UNITS * q + s
            g = v // 2
            if v % 2 == 0:
                pe.wait_ge(xbd_ready, 2 * u + g + 1)
                pe.wait_ge(prod_ready, 2 * u + g + 1)
            for p in range(2):
                wait(pe, t_copied[p], 4 * u + v - 1)
            for n in range(GROUP // 2):
                for p in range(2):
                    b = (v % 2) * GROUP + p * GROUP // 2 + n
                    last = pe.matmul(bank(TG + 2 * (v % 2) + n // 2, (n % 2) * 2 * COLS, 2 * COLS, D * p, D),
                                     xbd[s % 2][:, (g * SUB + b) * 2 * M:(g * SUB + b + 1) * 2 * M],
                                     prod[2 * (s % 2) + g][:, 2 * b * COLS:2 * (b + 1) * COLS],
                                     start=True, stop=True)
            last.then_inc(t_done, 1)

        def copy_t(eng, copy, p, q, t_at, s, v):
            u = UNITS * q + s
            if s == 0 and v == 0:
                wait(eng, t_free, q)
            eng.wait_ge(t_done, 4 * u + v + 1)
            for e in range(2):
                src = at(psum, (TG + 2 * (v % 2)) * BANK + e * COLS, [[BANK, 2], [2 * COLS, 2], [1, COLS]], D * p, D)
                c = s * UNIT + v * GROUP + p * GROUP // 2
                dst = t_sb[D * e:D * (e + 1), bass.ds(t_at + c, 1)]
                dst = bass.AP(dst.tensor, dst.offset, [list(dst.ap[0]), [2, 2], [1, 2], [CHUNK, COLS]])
                last = copy(dst, src)
            last.then_inc(t_copied[p], 1)

        def act_copy_t(act, q, t_at, s, v, p=0):
            copy_t(act, lambda o, i: act.activation(o, i, ACT.Copy), p, q, t_at, s, v)

        def dve_copy_t(dve, q, t_at, s, v):
            copy_t(dve, dve.tensor_copy, 1, q, t_at, s, v)

        def act_xx(act, q, s, g):
            u = UNITS * q + s
            act.wait_ge(xt_done, u + 1)
            wait(act, prod_ready, 2 * (u - 2) + g + 1)
            copy_xx(act, q, s, g)

        def act_xbd(act, q, s, g):
            u = UNITS * q + s
            act.wait_ge(xt_done, u + 1)
            wait(act, t_done, 4 * (u - 2) + 2 * (g + 1))
            copy_xbd(act, q, s, g)

        def products(dve, q, s, g, part=None):
            u = UNITS * q + s
            p, x, x0 = prod[2 * (s % 2) + g], xx[s % 2], g * SUB * 2 * HALF
            row, xrow = 2 * COLS, 2 * HALF
            if part in (None, 0):
                dve.wait_ge(xx_ready, 2 * u + g + 1)
                wait(dve, t_done, 4 * (u - 2) + 2 * (g + 1))
            for e in range(2):
                if part in (None, e):
                    dve.tensor_tensor(at(p, e * COLS, [[row, SUB], [HALF, SHIFTS], [1, HALF]]),
                                      at(x, x0, [[xrow, SUB], [0, SHIFTS], [1, HALF]]),
                                      at(x, x0 + SHIFTS * e, [[xrow, SUB], [1, SHIFTS], [1, HALF]]), ALU.mult)
            if part in (None, 2):
                dve.tensor_tensor(at(p, SHIFTS * HALF, [[row, SUB], [COLS, 2], [1, LAST]]),
                                  at(x, x0, [[xrow, SUB], [LAST, 2], [1, LAST]]),
                                  at(x, x0 + HALF // 2, [[xrow, SUB], [LAST, 2], [1, LAST]]), ALU.mult)
                dve.tensor_copy(at(p, PAIRS, [[row, SUB], [COLS, 2], [1, GRAM]]),
                                at(x, x0, [[xrow, SUB], [GRAM, 2], [1, GRAM]])).then_inc(prod_ready, 1)

        def weight_products(pe, x):
            if x % (M // W1_CHUNKS) == 0:
                pe.wait_ge(w1_in_sb[x // (M // W1_CHUNKS)], 16)
            k, y = divmod(x, HALF)
            w = w1_sb[:, x * O:(x + 1) * O]
            if x == 0:
                pe.wait_ge(w0_ready, 1)
            wait(pe, u_cross, x - 1)
            pe.matmul(bank(W_BANKS[2 * x % 3], 0, 4 * VCOLS), w, w0p_sb[:, :], start=True, stop=True)\
                .then_inc(u_done, 1)
            c = (2 * k * HALF + y) * HALF
            if x == 0:
                pe.wait_ge(w0_ready, 2)
            wait(pe, u_pairs, x)
            pe.matmul(bank(W_BANKS[(2 * x + 1) % 3], 0, HALF * HALF), w, w0x_sb[:, c:c + HALF * HALF],
                      start=True, stop=True).then_inc(u_done, 1)

        def copy_pairs(act, x):
            act.wait_ge(u_done, 2 * x + 1)
            src = at(psum, W_BANKS[2 * x % 3] * BANK, [[VCOLS, 4], [1, VCOLS]])
            act.activation(at(t_sb, coef_t_at + x, [[M, 4], [128, VCOLS]]), src, ACT.Copy).then_inc(u_pairs, 1)

        def copy_cross(dve, x):
            dve.wait_ge(u_done, 2 * x + 2)
            dve.tensor_copy(cross[:, x * HALF * HALF:(x + 1) * HALF * HALF],
                            bank(W_BANKS[(2 * x + 1) % 3], 0, HALF * HALF)).then_inc(u_cross, 1)

        XS, KS = HALF * HALF, HALF ** 3

        def add_cross(eng, e, i, k, dims, src, src_dims):
            dst = coef_t_at + i * 128 + 2 * M * e + HALF + HALF * k
            return eng.tensor_tensor(at(t_sb, dst, dims), at(t_sb, dst, dims), at(cross, src, src_dims), ALU.add)

        def fold_first(eng, shifts, step):
            for e in range(2):
                mine = [s for s in shifts if s // SHIFTS == e]
                for k in range(2 if mine else 0):
                    last = add_cross(eng, e, mine[0] % SHIFTS * HALF, k,
                                     [[HALF * 128, len(mine)], [128, HALF], [1, HALF]],
                                     k * KS + mine[0] * HALF, [[HALF, len(mine)], [XS, HALF], [1, HALF]])
            for e in range(2 if 0 in shifts else 0):
                last = add_cross(eng, e, SHIFTS * HALF, 0, [[HALF, 2], [128, LAST], [1, HALF]],
                                 LAST * e * XS + HALF // 2 * HALF, [[KS, 2], [XS, LAST], [1, HALF]])
            last.then_inc(step, 1)

        def fold_second(eng, shifts, step):
            for s in shifts:
                e, i = divmod(s, SHIFTS)
                for h, n in ((0, HALF - s), (HALF - s, s)) if s else ():
                    last = add_cross(eng, e, i * HALF + h, 0, [[HALF, 2], [128, n], [1, HALF]],
                                     (h + s) % HALF * XS + (HALF - s) * HALF, [[KS, 2], [XS, n], [1, HALF]])
            for e in range(2 if 0 in shifts else 0):
                last = add_cross(eng, e, SHIFTS * HALF, 0, [[HALF, 2], [128, LAST], [1, HALF]],
                                 (HALF // 2 + LAST * e) * XS + HALF // 2 * HALF, [[KS, 2], [XS, LAST], [1, HALF]])
            last.then_inc(step, 1)

        def transpose_coef(pe, n):
            if n == 0:
                pe.wait_ge(fold_step, 2)
            if n == HALF // 4:
                pe.wait_ge(fold_step, 3)
                pe.wait_ge(pool_step, 2)
            if n >= 4:
                pe.wait_ge(coef_ready[COPIER[n - 4]], COPIER[:n - 3].count(COPIER[n - 4]))
            for i in range(4 * n, min(4 * n + 4, VCOLS)):
                c = coef_t_at + i * 128
                last = pe.matmul(bank(C_BANKS[n % 4], (i - 4 * n) * 128, 128), t_sb[:, c:c + 128],
                                 ident[:, :], is_transpose=True, start=True, stop=True)
            last.then_inc(coef_tr if n < V_GROUPS - 1 else t_free, 1)

        def copy_coef(eng, copy, n):
            if n == COPIER.index(COPIER[n]):
                eng.wait_ge(fold_step, 3)
                eng.wait_ge(pool_step, 2)
            c = min(4, VCOLS - 4 * n) * O
            if n < V_GROUPS - 1:
                eng.wait_ge(coef_tr, n + 1)
            else:
                eng.wait_ge(t_free, 1)
            copy(coef[:, 4 * n * O:4 * n * O + c], bank(C_BANKS[n % 4], 0, c)).then_inc(coef_ready[COPIER[n]], 1)

        CIN = [(ACC + 1, w0g_sb, i * O, (PAIRS + i) * CHUNK, i == 0, i == GRAM - 1) for i in range(GRAM)]
        CIN += [(ACC, coef, i * O, (i if i < PAIRS else COLS - 1) * CHUNK, i == 0, i == VCOLS - 1) for i in range(VCOLS)]

        def cin(pe, c, t_at, part):
            if part == 0:
                for p in range(2):
                    pe.wait_ge(t_copied[p], (c + 1) * UNITS * 4)
                wait(pe, acc_free, 2 * c)
            for n, w, wc, tc, first, end in CIN[len(CIN) * part // 4:len(CIN) * (part + 1) // 4]:
                last = pe.matmul(bank(n, 0, CHUNK), w[:, wc:wc + O], t_sb[:, bass.ds(t_at + tc, CHUNK)],
                                 start=first, stop=end)
                if end:
                    last.then_inc(cin1_done if n == ACC + 1 else t_free, 1)

        def copy_z(act, q):
            for n, done in ((1, cin1_done), (0, t_free)):
                act.wait_ge(done, q + 2 - n)
                act.activation(w1_sb[:, bass.ds(z_at + (1 - n) * B + q * CHUNK, CHUNK)], bank(ACC + n, 0, CHUNK),
                               ACT.Identity, bias=cin_bias[:, 3 - n:4 - n]).then_inc(acc_free, 1)

        def chunk(step, q, far, final=False):
            for s in range(UNITS):
                ahead = (q, s + far) if s + far < UNITS else (None if final else (q + 1, s + far - UNITS))
                step(q, s, ahead)

        @block.gpsimd
        def _(pool):
            pool.memset(ident[:, :], 0.0).then_inc(ident_zero, 1)
            pool.wait_ge(ident_zero, 1)
            pool.affine_select(out=ident[:, :], in_=ident[:, :], compare_op=ALU.not_equal, fill=1.0, base=0,
                               pattern=[[-1, 128]], channel_multiplier=1).then_inc(ident_ready, 1)
            pool.wait_ge(idx_ready, 1)
            for u in range(CHUNKS * UNITS):
                s = u % UNITS
                if u >= UNITS:
                    pool.wait_ge(xt_done, u - UNITS + 1)
                for n in range(TILES):
                    c = (s * TILES + n) * D
                    g = u * TILES + n
                    if g == FOLD_AT:
                        pool.wait_ge(u_pairs, M)
                        pool.wait_ge(u_cross, M)
                        fold_first(pool, POOL_SHIFTS, pool_step)
                        pool.wait_ge(pool_step, 1)
                        fold_second(pool, POOL_SHIFTS, pool_step)
                    pool.indirect_dma_start(rows[:, c:c + D], None, table[:, :],
                                            bass.IndirectOffsetOnAxis(ap=idx[:, g:g + 1], axis=0))\
                        .then_inc(gathered[s], 16)

        @block.tensor
        def _(pe):
            pe.wait_ge(ident_ready, 1)
            def weights(start, end):
                for x in range(start, end):
                    weight_products(pe, x)

            weights(0, 7)
            transpose_rows(pe, 0, 0)
            weights(7, 14)
            transpose_rows(pe, 0, 1)
            pe.wait_ge(fills_ready, 1)
            for s, (x0, x1, x2, x3) in enumerate(W_PARTS):
                t_group(pe, 0, s, 0)
                t_group(pe, 0, s, 1)
                weights(x0, x1)
                t_group(pe, 0, s, 2)
                weights(x1, x2)
                t_group(pe, 0, s, 3)
                weights(x2, x3)
                transpose_rows(pe, (s + 2) // UNITS, (s + 2) % UNITS)
            for v in range(4):
                t_group(pe, 0, 3, v)
            pe.wait_ge(u_pairs, M)
            pe.wait_ge(u_cross, M)
            for p in range(2):
                pe.wait_ge(t_copied[p], UNITS * 4)
            for n in range(V_GROUPS):
                transpose_coef(pe, n)
                if n == V_GROUPS // 2:
                    transpose_rows(pe, 1, 1)
            for n in range(2):
                pe.wait_ge(coef_ready[n], COPIER.count(n))
            pe.wait_ge(w0g_in_sb, 16)

            def step(q, s, ahead, last_at):
                for v in range(4):
                    t_group(pe, q, s, v)
                    if v == 1 and ahead:
                        transpose_rows(pe, *ahead)
                cin(pe, q - 1, last_at, s)

            with pe.Fori(1, CHUNKS - 1) as q:
                t_last = pe.snap((q + 1) % 2 * (COLS * CHUNK))
                chunk(lambda q, s, ahead: step(q, s, ahead, t_last), q, 2)
            c = CHUNKS - 1
            chunk(lambda q, s, ahead: step(q, s, ahead, (c - 1) % 2 * COLS * CHUNK), c, 2, final=True)
            pe.wait_ge(top_in_sb, TOP_DMAS * 16)
            pe.wait_ge(xx_ready, 2 * CHUNKS * UNITS)
            pe.wait_ge(xbd_ready, 2 * CHUNKS * UNITS)
            for p in range(2):
                pe.wait_ge(t_copied[p], CHUNKS * UNITS * 4 - 1)
            for j in range(TOP1 // 128):
                pe.matmul(bank(L1 + j), w1_sb[32 * j:32 * j + DENSE, top1d_at:top1d_at + 128],
                          w1_sb[32 * j:32 * j + DENSE, dense_at:dense_at + B], start=True, stop=False)
            for part in range(4):
                cin(pe, c, c % 2 * COLS * CHUNK, part)
            for n in range(2):
                pe.wait_ge(acc_free, 2 * CHUNKS - 1 + n)
                for j in range(TOP1 // 128):
                    c = top1_at + n * TOP1 + 128 * j
                    last = pe.matmul(bank(L1 + j), w1_sb[:, c:c + 128], w1_sb[:, z_at + n * B:z_at + (n + 1) * B],
                                     start=False, stop=(n == 1))
                    if n == 1:
                        last.then_inc(l1_done, 1)
            for j in range(TOP2 // 128):
                for n in range(TOP1 // 128):
                    if j == 0:
                        pe.wait_ge(l1_ready, n + 1)
                    c = top2_at + n * TOP2 + 128 * j
                    last = pe.matmul(bank(ACC + j), w1_sb[:, c:c + 128],
                                     hid1[n // 2][:, n % 2 * B:(n % 2 + 1) * B], start=(n == 0), stop=(n == 3))
                last.then_inc(l2_done, 1)
            for n in range(TOP2 // 128):
                pe.wait_ge(l2_ready, n + 1)
                for j in range(4):
                    c = n * B + j * B // 4
                    last = pe.matmul(bank(L3, 0, B // 4, 32 * j, 1), top3_sb[:, n:n + 1],
                                     hid2[:, c:c + B // 4], start=(n == 0), stop=(n == 1), tile_position=(0, 32 * j))
            last.then_inc(l3_done, 1)

        @block.scalar
        def _(act):
            def pairs(start, end):
                for x in range(start, end):
                    copy_pairs(act, x)

            act.dma_start(at(t_sb, pair_in, [[1, 2 * 4 * VCOLS]]), w0p).then_inc(w0p_in_sb, 16)
            act.dma_start(at(t_sb, cross_in, [[1, 4 * HALF * HALF]]), w0x).then_inc(w0x_in_sb, 16)
            pairs(0, 8)
            act_xx(act, 0, 0, 0)
            pairs(8, 9)
            act_xx(act, 0, 0, 1)
            pairs(9, 10)
            act.wait_ge(fills_ready, 1)
            act_xbd(act, 0, 0, 0)
            pairs(10, 11)
            act_xbd(act, 0, 0, 1)
            pairs(11, 14)
            for s, (x0, x1, x2, x3) in enumerate(W_PARTS):
                act_xx(act, 0, s + 1, 0)
                act_copy_t(act, 0, 0, s, 0)
                act_copy_t(act, 0, 0, s, 1)
                act_xx(act, 0, s + 1, 1)
                pairs(x0, x1)
                act_copy_t(act, 0, 0, s, 2)
                pairs(x1, x2)
                act_xbd(act, 0, s + 1, 0)
                act_copy_t(act, 0, 0, s, 3)
                pairs(x2, x2 + 1)
                act_xbd(act, 0, s + 1, 1)
                pairs(x2 + 1, x3)
            for v in range(4):
                act_copy_t(act, 0, 0, 3, v)
                if v == 0:
                    act.wait_ge(t_copied[1], 3 * 4)
                act_copy_t(act, 0, 0, 3, v, p=1)
                if v % 2:
                    act_xx(act, 1, 0, v // 2)
            for g in range(2):
                act_xbd(act, 1, 0, g)
            for n in range(V_GROUPS):
                if COPIER[n] == 0:
                    copy_coef(act, lambda o, i: act.activation(o, i, ACT.Copy), n)
                if n == V_GROUPS // 2 + 3:
                    act_xx(act, 1, 1, 0)
                    act_xx(act, 1, 1, 1)
            act_xbd(act, 1, 1, 0)
            act_xbd(act, 1, 1, 1)

            def step(q, s, ahead, t_at):
                for v in range(4):
                    act_copy_t(act, q, t_at, s, v)
                    if v == 1 and ahead:
                        act_xx(act, *ahead, 0)
                if ahead:
                    act_xx(act, *ahead, 1)
                    act_xbd(act, *ahead, 0)
                    act_xbd(act, *ahead, 1)
                if s == UNITS - 1:
                    copy_z(act, q - 1)

            act.wait_ge(bias_ready, 1)
            act.wait_ge(u_done, 2 * M)
            with act.Fori(1, CHUNKS - 1) as q:
                t_at = act.snap(q % 2 * (COLS * CHUNK))
                chunk(lambda q, s, ahead: step(q, s, ahead, t_at), q, 2)
            c = CHUNKS - 1
            chunk(lambda q, s, ahead: step(q, s, ahead, c % 2 * COLS * CHUNK), c, 2, final=True)
            copy_z(act, c)
            for j in range(TOP1 // 128):
                act.wait_ge(l1_done, j + 1)
                act.activation(hid1[j // 2][:, j % 2 * B:(j % 2 + 1) * B], bank(L1 + j), ACT.Relu,
                               bias=top_bias[:, j:j + 1]).then_inc(l1_ready, 1)
            for j in range(TOP2 // 128):
                act.wait_ge(l2_done, j + 1)
                act.activation(hid2[:, j * B:(j + 1) * B], bank(ACC + j), ACT.Relu,
                               bias=top_bias[:, 4 + j:5 + j]).then_inc(l2_ready, 1)
            act.wait_ge(l3_done, 1)
            for j in range(2):
                last = act.activation(at(prod[3], 0, [[1, B // 4]], 32 * j, 1), bank(L3, 0, B // 4, 32 * j, 1), ACT.Copy)
            last.then_inc(l3_ready, 1)

        @block.vector
        def _(dve):
            dve.wait_ge(ids_in_sb, 32)
            n = idx.shape[1]
            dve.tensor_tensor(idx[:, :], at(t_sb, ids_in, [[1, n]]).bitcast(I32),
                              at(t_sb, base_in, [[1, n]]).bitcast(I32), ALU.add).then_inc(idx_ready, 1)
            dve.wait_ge(w0p_in_sb, 16)
            n = 4 * VCOLS
            dve.tensor_tensor(w0p_sb[:, :], t_sb[:, pair_in:pair_in + n], t_sb[:, pair_in + n:pair_in + 2 * n],
                              ALU.add).then_inc(w0_ready, 1)
            dve.wait_ge(w0x_in_sb, 16)
            n = HALF * HALF
            dve.tensor_tensor(at(w0x_sb, 0, [[2 * n, 2], [n, 2], [1, n]]), at(t_sb, cross_in, [[n, 2], [0, 2], [1, n]]),
                              at(t_sb, cross_in + 2 * n, [[n, 2], [0, 2], [1, n]]), ALU.add).then_inc(w0_ready, 1)
            def cross_copies(start, end):
                for x in range(start, end):
                    copy_cross(dve, x)

            for n in range(4):
                cross_copies(n, n + 1)
                half = UNIT * M
                dve.memset(xbd[n // 2][:, n % 2 * half:(n % 2 + 1) * half], 0.0)
                last = dve.memset(at(prod[n], COLS - 1, [[COLS, 2 * SUB]]), 1.0)
            last.then_inc(fills_ready, 1)
            dve.wait_ge(fills_ready, 1)
            cross_copies(4, 8)
            for n in range(6):
                products(dve, 0, 0, n // 3, n % 3)
                cross_copies(8 + n, 9 + n)
            for s, (x0, x1, x2, x3) in enumerate(W_PARTS):
                dve_copy_t(dve, 0, 0, s, 0)
                products(dve, 0, s + 1, 0, 0)
                dve_copy_t(dve, 0, 0, s, 1)
                cross_copies(x0, x1)
                products(dve, 0, s + 1, 0, 1)
                dve_copy_t(dve, 0, 0, s, 2)
                cross_copies(x1, x2)
                products(dve, 0, s + 1, 0, 2)
                products(dve, 0, s + 1, 1, 0)
                dve_copy_t(dve, 0, 0, s, 3)
                if x3 < M:
                    cross_copies(x2, x2 + 1)
                    products(dve, 0, s + 1, 1, 1)
                    cross_copies(x2 + 1, x3)
                else:
                    cross_copies(x2, x3)
                    products(dve, 0, s + 1, 1, 1)
                products(dve, 0, s + 1, 1, 2)
            dve.wait_ge(u_pairs, M)
            dve.wait_ge(u_cross, M)
            fold_first(dve, DVE_SHIFTS, fold_step)
            dve.wait_ge(fold_step, 1)
            fold_second(dve, (0, SHIFTS), fold_step)
            fold_second(dve, [s for s in DVE_SHIFTS if s % SHIFTS], fold_step)
            copies = [n for n in range(V_GROUPS) if COPIER[n] == 1]
            for n in range(6):
                products(dve, 1, 0, n // 3, n % 3)
                for m in copies[n:n + 1]:
                    copy_coef(dve, dve.tensor_copy, m)
            dve.wait_ge(t_copied[1], UNITS * 4)

            def step(q, s, ahead, t_at):
                for g in range(2):
                    dve_copy_t(dve, q, t_at, s, 2 * g)
                    dve_copy_t(dve, q, t_at, s, 2 * g + 1)
                    if ahead:
                        products(dve, *ahead, g)

            dve.wait_ge(small_in_sb, 32)
            dve.tensor_scalar(cin_bias[:, 2:4], cin_bias[:, 0:2], float(D), None, ALU.mult).then_inc(bias_ready, 1)
            with dve.Fori(1, CHUNKS - 1) as q:
                t_at = dve.snap(q % 2 * (COLS * CHUNK))
                chunk(lambda q, s, ahead: step(q, s, ahead, t_at), q, 1)
            c = CHUNKS - 1
            chunk(lambda q, s, ahead: step(q, s, ahead, c % 2 * COLS * CHUNK), c, 1, final=True)

            dve.wait_ge(l3_done, 1)
            for j in range(2, 4):
                last = dve.tensor_copy(at(prod[3], 0, [[1, B // 4]], 32 * j, 1), bank(L3, 0, B // 4, 32 * j, 1))
            last.then_inc(l3_ready, 1)


def _pairs():
    out = np.zeros((2, 2, PAIRS, 2), np.int64)
    for e in range(2):
        for k in range(2):
            at = [(h, (h + s) % HALF) for s in range(SHIFTS * e, SHIFTS * (e + 1)) for h in range(HALF)]
            at += [(h, h + HALF // 2) for h in range(LAST * e, LAST * (e + 1))]
            out[e, k] = np.array(at) + HALF * k
    return out.reshape(4, PAIRS, 2)


def kernel(**inputs):
    import concourse.bacc as bacc
    from concourse import mybir as _mybir
    from concourse.bass_utils import run_bass_kernel_spmd

    a = {name: np.asarray(x) for name, x in inputs.items()}
    tables = [a[f"tbl_{f}"] for f in range(M)]
    starts = np.cumsum([0] + [t.shape[0] for t in tables])[:-1].astype(np.int32)

    ids = a["ids"].reshape(CHUNKS * UNITS, 2, TILES // 2, PER_GATHER, M).transpose(3, 4, 0, 2, 1).reshape(128, -1)
    base = np.ascontiguousarray(np.broadcast_to(np.tile(starts, PER_GATHER)[:, None], ids.shape))

    w0 = a["L0_rec_W0"].reshape(O, M, M)
    w1 = a["L0_rec_W1"].reshape(O, M, O)
    pairs = _pairs()
    w0p = np.zeros((O, 2, 4, VCOLS), w0.dtype)
    w0p[:, 0, :, :PAIRS] = w0[:, pairs[..., 0], pairs[..., 1]]
    other = pairs[..., 0] != pairs[..., 1]
    w0p[:, 1, :, :PAIRS][:, other] = w0[:, pairs[..., 1], pairs[..., 0]][:, other]
    w0p[:, 0, 0, PAIRS] = a["L0_rec_b0"]
    lo, hi = slice(0, HALF), slice(HALF, M)
    w0x = np.stack([w0[:, lo, hi], w0[:, hi, lo], w0[:, hi, lo].transpose(0, 2, 1), w0[:, lo, hi].transpose(0, 2, 1)], axis=1)
    w0g = w0.reshape(O, M, 2, 2, GRAM).transpose(3, 2, 1, 4, 0).reshape(128, GRAM * O)

    arrays = {
        "table": np.concatenate(tables, axis=0),
        "ids": ids,
        "base": base,
        "w1t": w1.transpose(2, 1, 0).reshape(O, M * O),
        "w0p": w0p.reshape(O, -1),
        "w0x": w0x.reshape(O, -1),
        "w0g": w0g,
        "cin_b": np.stack([a["L0_rec_b0"], a["L0_rec_b1"]], axis=1),
        "top1": a["W_top1"][:2 * O].reshape(2, O, TOP1).transpose(1, 0, 2).reshape(O, -1),
        "top1d": a["W_top1"][2 * O:],
        "top2": a["W_top2"].reshape(4, 128, TOP2).transpose(1, 0, 2).reshape(128, -1),
        "top3": a["W_top3"].reshape(2, 128).T,
        "b_top": np.concatenate([a["b_top1"].reshape(4, 128), a["b_top2"].reshape(2, 128)], axis=0).T,
        "dense": a["dense_ctx"].T,
    }
    arrays = {name: np.ascontiguousarray(x) for name, x in arrays.items()}
    nc = bacc.Bacc("TRN2", target_bir_lowering=False, num_devices=1)
    args = [nc.dram_tensor(name, x.shape, _mybir.dt.from_np(x.dtype), kind="ExternalInput").ap()
            for name, x in arrays.items()]
    out = nc.dram_tensor("out", (4, B // 4), _mybir.dt.float32, kind="ExternalOutput").ap()
    build(nc, *args, out)
    r = run_bass_kernel_spmd(nc, [arrays], core_ids=[0])
    return r.results[0]["out"].reshape(B, 1)
```

```python
import concourse.bass as bass
from concourse import mybir
from contextlib import ExitStack
import numpy as np

B = 512
M = 32
D = 64
O = 128
HALF = M // 2
SHIFTS = 4
LAST = 4
PAIRS = SHIFTS * HALF + LAST
GRAM = HALF // 2
COLS = PAIRS + GRAM + 1
VCOLS = PAIRS + 1
UNIT = 32
SUB = UNIT // 2
GROUP = 8
UNITS = 4
CHUNK = UNIT * UNITS
CHUNKS = B // CHUNK
PER_GATHER = 128 // M
TILES = UNIT // PER_GATHER
TOP1, TOP2 = 512, 256
DENSE = 16
BANK = 512
W1_PARTS = (0, 2, 8, 16, 24, 32)


def build(nc, table, ids, base, w1t, w0p, w0x, w0g, cin_b, top1, top1d, top2, top3, b_top, dense, out):
    F32, I32 = mybir.dt.float32, mybir.dt.int32
    ALU, ACT = mybir.AluOpType, mybir.ActivationFunctionType

    with ExitStack() as ctx:
        def sb(name, cols, dt=F32):
            return ctx.enter_context(nc.sbuf_tensor(name, [128, cols], dt))

        def sem(name):
            return ctx.enter_context(nc.semaphore(name))

        def at(t, col, dims, part=0, parts=128):
            row = t[:, :].ap[0][0]
            return bass.AP(t[:, :].tensor, part * row + col, [[row, parts]] + dims)

        t_sb = sb("t_sb", 2 * COLS * CHUNK)
        coef = sb("coef", VCOLS * O)
        coef_t_at = COLS * CHUNK
        rows = sb("rows", UNITS * TILES * D)
        prod = [sb(f"prod{n}", SUB * 2 * COLS) for n in range(4)]
        xbd = [sb(f"xbd{n}", UNIT * 2 * M) for n in range(2)]
        xx = [sb(f"xx{n}", UNIT * 2 * HALF) for n in range(2)]
        w1_sb = sb("w1_sb", M * O)
        w0p_sb = sb("w0p_sb", 4 * VCOLS)
        w0x_sb = sb("w0x_sb", 2 * 2 * HALF * HALF)
        w0g_sb = w0x_sb
        ident = sb("ident", 128)
        cin_bias = sb("cin_bias", 4)
        top_bias = sb("top_bias", 6)
        top3_sb = sb("top3_sb", 2)
        idx = sb("idx", UNITS * CHUNKS * TILES, I32)

        cross = coef
        pair_in, cross_in, base_in = 0, 2 * 4 * VCOLS, 2 * 4 * VCOLS + 4 * HALF * HALF
        ids_in = base_in + idx.shape[1]
        top1_at, top1d_at = 0, 2 * TOP1
        top2_at = top1d_at + 128
        dense_at = top2_at + 4 * TOP2
        z_at = dense_at + B
        hid1, hid2 = prod[0:2], prod[2]

        psum = ctx.enter_context(nc.psum_tensor("psum", [128, 8 * BANK], F32))

        def bank(n, col=0, cols=BANK, part=0, parts=128):
            return psum[part:part + parts, n * BANK + col:n * BANK + col + cols]

        XT = 0
        SPARE = 1
        TG = 2
        ACC = 6
        L1 = XT
        L3 = TG + 2
        C_BANKS = (ACC, ACC + 1, SPARE, TG)
        W_BANKS = (ACC, ACC + 1, SPARE)

        ids_in_sb = sem("ids_in_sb")
        w0p_in_sb, w0x_in_sb = sem("w0p_in_sb"), sem("w0x_in_sb")
        w1_in_sb = [sem(f"w1_in_sb{n}") for n in range(len(W1_PARTS) - 1)]
        small_in_sb = sem("small_in_sb")
        top_in_sb = sem("top_in_sb")
        w0g_in_sb = sem("w0g_in_sb")
        idx_ready = sem("idx_ready")
        ident_zero, ident_ready = sem("ident_zero"), sem("ident_ready")
        gathered = [sem(f"gathered{s}") for s in range(UNITS)]
        xt_done = sem("xt_done")
        xx_ready = sem("xx_ready")
        xbd_ready = sem("xbd_ready")
        prod_ready = sem("prod_ready")
        fills_ready = sem("fills_ready")
        w0_ready = sem("w0_ready")
        bias_ready = sem("bias_ready")
        t_done = sem("t_done")
        t_copied = [sem(f"t_copied{p}") for p in range(2)]
        cin1_done = sem("cin1_done")
        t_free = sem("t_free")
        u_done = sem("u_done")
        u_pairs = sem("u_pairs")
        u_cross = sem("u_cross")
        fold_step = sem("fold_step")
        pool_step = sem("pool_step")
        pool_prod = sem("pool_prod")
        coef_tr = sem("coef_tr")
        coef_ready = [sem(f"coef_ready{n}") for n in range(2)]
        acc_free = sem("acc_free")
        l1_done, l1_ready = sem("l1_done"), sem("l1_ready")
        l2_done, l2_ready = sem("l2_done"), sem("l2_ready")
        l3_done, l3_ready = sem("l3_done"), sem("l3_ready")
        stored = sem("stored")

        W_PARTS = [(16, 17, 19, 21), (21, 22, 24, 26), (26, 28, 30, 32)]

        TOP_DMAS = 3 + 2 * TOP1 // 128
        W_ROWS = 10
        V_GROUPS = -(-VCOLS // 4)
        COPIER = [n % 3 // 2 for n in range(V_GROUPS)]
        DVE_SHIFTS, POOL_SHIFTS = range(0, 6), range(6, 8)
        FOLD_AT = 6 * TILES + 2

        def wait(eng, s, n):
            if not isinstance(n, int) or n > 0:
                eng.wait_ge(s, n)

        block = ctx.enter_context(nc.Block())

        @block.sync
        def _(sp):
            sp.dma_start(at(t_sb, ids_in, [[1, idx.shape[1]]]).bitcast(I32), ids).then_inc(ids_in_sb, 16)
            sp.dma_start(at(t_sb, pair_in, [[1, 2 * 4 * VCOLS]]), w0p).then_inc(w0p_in_sb, 16)
            for n, (x0, x1) in enumerate(zip(W1_PARTS, W1_PARTS[1:])):
                sp.dma_start(w1_sb[:, x0 * O:x1 * O], w1t[:, x0 * O:x1 * O]).then_inc(w1_in_sb[n], 16)
            sp.dma_start(cin_bias[:, 0:2], cin_b).then_inc(small_in_sb, 16)
            sp.dma_start(top_bias[:, :], b_top).then_inc(small_in_sb, 16)
            sp.wait_ge(u_done, 2 * M)
            sp.dma_start(w0g_sb[:, :], w0g).then_inc(w0g_in_sb, 16)
            sp.dma_start(w1_sb[:, top1_at:top1_at + 2 * TOP1], top1).then_inc(top_in_sb, 16)
            sp.dma_start(w1_sb[:, top2_at:top2_at + 4 * TOP2], top2).then_inc(top_in_sb, 16)
            sp.dma_start(top3_sb[:, :], top3).then_inc(top_in_sb, 16)
            for j in range(TOP1 // 128):
                sp.dma_start(w1_sb[32 * j:32 * j + DENSE, top1d_at:top1d_at + 128], top1d[:, 128 * j:128 * (j + 1)])\
                    .then_inc(top_in_sb, 16)
                sp.dma_start(w1_sb[32 * j:32 * j + DENSE, dense_at:dense_at + B], dense).then_inc(top_in_sb, 16)
            sp.wait_ge(l3_ready, 2)
            row = prod[3][:, :].ap[0][0]
            sp.dma_start(out, bass.AP(prod[3][:, :].tensor, 0, [[32 * row, 4], [1, B // 4]])).then_inc(stored, 16)
            sp.wait_ge(stored, 16)


        def transpose_rows(pe, q, s):
            u = UNITS * q + s
            pe.wait_ge(gathered[s], (q + 1) * 16 * TILES)
            wait(pe, xx_ready, 2 * u)
            wait(pe, xbd_ready, 2 * u)
            for t in range(TILES // 2):
                c = (s * TILES + 2 * t) * D
                last = pe.matmul(bank(XT, 128 * t, 128), rows[:, c:c + 2 * D], ident[:, :],
                                 is_transpose=True, start=True, stop=True)
            last.then_inc(xt_done, 1)

        def copy_xx(act, q, s, g, ks):
            for k in ks:
                src = at(psum, XT * BANK + HALF * k, [[M, SUB], [0, 2], [1, HALF]], D * g, D)
                dst = at(xx[s % 2], g * SUB * 2 * HALF, [[2 * HALF, SUB], [HALF, 2], [1, HALF]], D * k, D)
                last = act.activation(dst, src, ACT.Copy)
            if k == 1:
                last.then_inc(xx_ready, 1)

        def copy_xbd(act, q, s, g, ks):
            for k in ks:
                src = at(psum, XT * BANK, [[M, SUB], [1, M]], D * g, D)
                dst = at(xbd[s % 2], g * SUB * 2 * M + M * k, [[2 * M, SUB], [1, M]], D * k, D)
                last = act.activation(dst, src, ACT.Copy)
            if k == 1:
                last.then_inc(xbd_ready, 1)

        def t_group(pe, q, s, v):
            u = UNITS * q + s
            g = v // 2
            if v % 2 == 0:
                pe.wait_ge(xbd_ready, 2 * u + g + 1)
                pe.wait_ge(prod_ready, 2 * u + g + 1)
            for p in range(2):
                wait(pe, t_copied[p], 4 * u + v - 1)
            for n in range(GROUP // 2):
                for p in range(2):
                    b = (v % 2) * GROUP + p * GROUP // 2 + n
                    last = pe.matmul(bank(TG + 2 * (v % 2) + n // 2, (n % 2) * 2 * COLS, 2 * COLS, D * p, D),
                                     xbd[s % 2][:, (g * SUB + b) * 2 * M:(g * SUB + b + 1) * 2 * M],
                                     prod[2 * (s % 2) + g][:, 2 * b * COLS:2 * (b + 1) * COLS],
                                     start=True, stop=True)
            last.then_inc(t_done, 1)

        def copy_t(eng, copy, p, q, t_at, s, v):
            u = UNITS * q + s
            if s == 0 and v == 0:
                wait(eng, t_free, q)
            eng.wait_ge(t_done, 4 * u + v + 1)
            for e in range(2):
                src = at(psum, (TG + 2 * (v % 2)) * BANK + e * COLS, [[BANK, 2], [2 * COLS, 2], [1, COLS]], D * p, D)
                c = s * UNIT + v * GROUP + p * GROUP // 2
                dst = t_sb[D * e:D * (e + 1), bass.ds(t_at + c, 1)]
                dst = bass.AP(dst.tensor, dst.offset, [list(dst.ap[0]), [2, 2], [1, 2], [CHUNK, COLS]])
                last = copy(dst, src)
            last.then_inc(t_copied[p], 1)

        def act_copy_t(act, q, t_at, s, v, p=0):
            copy_t(act, lambda o, i: act.activation(o, i, ACT.Copy), p, q, t_at, s, v)

        def dve_copy_t(dve, q, t_at, s, v):
            copy_t(dve, dve.tensor_copy, 1, q, t_at, s, v)

        def act_xx(act, q, s, g, ks=(0, 1)):
            u = UNITS * q + s
            act.wait_ge(xt_done, u + 1)
            wait(act, prod_ready, 2 * (u - 2) + g + 1)
            copy_xx(act, q, s, g, ks)

        def act_xbd(act, q, s, g, ks=(0, 1)):
            u = UNITS * q + s
            act.wait_ge(xt_done, u + 1)
            wait(act, t_done, 4 * (u - 2) + 2 * (g + 1))
            copy_xbd(act, q, s, g, ks)

        def products(dve, q, s, g, part=None, first=0):
            u = UNITS * q + s
            p, x, x0 = prod[2 * (s % 2) + g], xx[s % 2], g * SUB * 2 * HALF
            row, xrow = 2 * COLS, 2 * HALF
            if part in (None, first):
                dve.wait_ge(xx_ready, 2 * u + g + 1)
                wait(dve, t_done, 4 * (u - 2) + 2 * (g + 1))
            for e in range(2):
                if part in (None, e):
                    last = dve.tensor_tensor(at(p, e * COLS, [[row, SUB], [HALF, SHIFTS], [1, HALF]]),
                                             at(x, x0, [[xrow, SUB], [0, SHIFTS], [1, HALF]]),
                                             at(x, x0 + SHIFTS * e, [[xrow, SUB], [1, SHIFTS], [1, HALF]]), ALU.mult)
            if part in (None, 2):
                dve.tensor_tensor(at(p, SHIFTS * HALF, [[row, SUB], [COLS, 2], [1, LAST]]),
                                  at(x, x0, [[xrow, SUB], [LAST, 2], [1, LAST]]),
                                  at(x, x0 + HALF // 2, [[xrow, SUB], [LAST, 2], [1, LAST]]), ALU.mult)
                dve.tensor_copy(at(p, PAIRS, [[row, SUB], [COLS, 2], [1, GRAM]]),
                                at(x, x0, [[xrow, SUB], [GRAM, 2], [1, GRAM]])).then_inc(prod_ready, 1)
            else:
                return last

        def weight_products(pe, x):
            if x in W1_PARTS:
                pe.wait_ge(w1_in_sb[W1_PARTS.index(x)], 16)
            k, y = divmod(x, HALF)
            w = w1_sb[:, x * O:(x + 1) * O]
            if x == 0:
                pe.wait_ge(w0_ready, 1)
            wait(pe, u_cross, x - 1)
            pe.matmul(bank(W_BANKS[2 * x % 3], 0, 4 * VCOLS), w, w0p_sb[:, :], start=True, stop=True)\
                .then_inc(u_done, 1)
            c = (2 * k * HALF + y) * HALF
            if x == 0:
                pe.wait_ge(w0_ready, 2)
            wait(pe, u_pairs, x)
            pe.matmul(bank(W_BANKS[(2 * x + 1) % 3], 0, HALF * HALF), w, w0x_sb[:, c:c + HALF * HALF],
                      start=True, stop=True).then_inc(u_done, 1)

        def copy_pairs(act, x):
            act.wait_ge(u_done, 2 * x + 1)
            src = at(psum, W_BANKS[2 * x % 3] * BANK, [[VCOLS, 4], [1, VCOLS]])
            act.activation(at(t_sb, coef_t_at + x, [[M, 4], [128, VCOLS]]), src, ACT.Copy).then_inc(u_pairs, 1)

        def copy_cross(dve, x):
            dve.wait_ge(u_done, 2 * x + 2)
            dve.tensor_copy(cross[:, x * HALF * HALF:(x + 1) * HALF * HALF],
                            bank(W_BANKS[(2 * x + 1) % 3], 0, HALF * HALF)).then_inc(u_cross, 1)

        XS, KS = HALF * HALF, HALF ** 3

        def add_cross(eng, e, i, k, dims, src, src_dims):
            dst = coef_t_at + i * 128 + 2 * M * e + HALF + HALF * k
            return eng.tensor_tensor(at(t_sb, dst, dims), at(t_sb, dst, dims), at(cross, src, src_dims), ALU.add)

        def fold_first(eng, shifts, step):
            for e in range(2):
                mine = [s for s in shifts if s // SHIFTS == e]
                for k in range(2 if mine else 0):
                    last = add_cross(eng, e, mine[0] % SHIFTS * HALF, k,
                                     [[HALF * 128, len(mine)], [128, HALF], [1, HALF]],
                                     k * KS + mine[0] * HALF, [[HALF, len(mine)], [XS, HALF], [1, HALF]])
            for e in range(2 if 0 in shifts else 0):
                last = add_cross(eng, e, SHIFTS * HALF, 0, [[HALF, 2], [128, LAST], [1, HALF]],
                                 LAST * e * XS + HALF // 2 * HALF, [[KS, 2], [XS, LAST], [1, HALF]])
            last.then_inc(step, 1)

        def fold_second(eng, shifts, step):
            for s in shifts:
                e, i = divmod(s, SHIFTS)
                for h, n in ((0, HALF - s), (HALF - s, s)) if s else ():
                    last = add_cross(eng, e, i * HALF + h, 0, [[HALF, 2], [128, n], [1, HALF]],
                                     (h + s) % HALF * XS + (HALF - s) * HALF, [[KS, 2], [XS, n], [1, HALF]])
            for e in range(2 if 0 in shifts else 0):
                last = add_cross(eng, e, SHIFTS * HALF, 0, [[HALF, 2], [128, LAST], [1, HALF]],
                                 (HALF // 2 + LAST * e) * XS + HALF // 2 * HALF, [[KS, 2], [XS, LAST], [1, HALF]])
            last.then_inc(step, 1)

        def transpose_coef(pe, n):
            if n == 0:
                pe.wait_ge(fold_step, 2)
            if n == HALF // 4:
                pe.wait_ge(fold_step, 3)
                pe.wait_ge(pool_step, 2)
            if n >= 4:
                pe.wait_ge(coef_ready[COPIER[n - 4]], COPIER[:n - 3].count(COPIER[n - 4]))
            for i in range(4 * n, min(4 * n + 4, VCOLS)):
                c = coef_t_at + i * 128
                last = pe.matmul(bank(C_BANKS[n % 4], (i - 4 * n) * 128, 128), t_sb[:, c:c + 128],
                                 ident[:, :], is_transpose=True, start=True, stop=True)
            last.then_inc(coef_tr if n < V_GROUPS - 1 else t_free, 1)

        def copy_coef(eng, copy, n):
            if n == COPIER.index(COPIER[n]):
                eng.wait_ge(fold_step, 3)
                eng.wait_ge(pool_step, 2)
            c = min(4, VCOLS - 4 * n) * O
            if n < V_GROUPS - 1:
                eng.wait_ge(coef_tr, n + 1)
            else:
                eng.wait_ge(t_free, 1)
            copy(coef[:, 4 * n * O:4 * n * O + c], bank(C_BANKS[n % 4], 0, c)).then_inc(coef_ready[COPIER[n]], 1)

        CIN = [(ACC + 1, w0g_sb, i * O, (PAIRS + i) * CHUNK, i == 0, i == GRAM - 1) for i in range(GRAM)]
        CIN += [(ACC, coef, i * O, (i if i < PAIRS else COLS - 1) * CHUNK, i == 0, i == VCOLS - 1) for i in range(VCOLS)]

        def cin(pe, c, t_at, part):
            if part == 0:
                for p in range(2):
                    pe.wait_ge(t_copied[p], (c + 1) * UNITS * 4)
                wait(pe, acc_free, 2 * c)
                for n in range(2):
                    pe.wait_ge(coef_ready[n], COPIER.count(n))
            for n, w, wc, tc, first, end in CIN[len(CIN) * part // 4:len(CIN) * (part + 1) // 4]:
                last = pe.matmul(bank(n, 0, CHUNK), w[:, wc:wc + O], t_sb[:, bass.ds(t_at + tc, CHUNK)],
                                 start=first, stop=end)
                if end:
                    last.then_inc(cin1_done if n == ACC + 1 else t_free, 1)

        def copy_z(act, q):
            for n, done in ((1, cin1_done), (0, t_free)):
                act.wait_ge(done, q + 2 - n)
                act.activation(w1_sb[:, bass.ds(z_at + (1 - n) * B + q * CHUNK, CHUNK)], bank(ACC + n, 0, CHUNK),
                               ACT.Identity, bias=cin_bias[:, 3 - n:4 - n]).then_inc(acc_free, 1)

        def chunk(step, q, final=False):
            for s in range(UNITS):
                step(q, s, [(q, s + n) if s + n < UNITS else (None if final else (q + 1, s + n - UNITS))
                            for n in range(3)])

        @block.gpsimd
        def _(pool):
            pool.memset(ident[:, :], 0.0).then_inc(ident_zero, 1)
            pool.wait_ge(ident_zero, 1)
            pool.affine_select(out=ident[:, :], in_=ident[:, :], compare_op=ALU.not_equal, fill=1.0, base=0,
                               pattern=[[-1, 128]], channel_multiplier=1).then_inc(ident_ready, 1)
            pool.wait_ge(idx_ready, 1)
            for u in range(CHUNKS * UNITS):
                s = u % UNITS
                if u >= UNITS:
                    pool.wait_ge(xt_done, u - UNITS + 1)
                for n in range(TILES):
                    c = (s * TILES + n) * D
                    g = u * TILES + n
                    if g == FOLD_AT:
                        products(pool, 0, 3, 1, 0)
                        products(pool, 0, 3, 1, 1).then_inc(pool_prod, 1)
                        pool.wait_ge(u_pairs, M)
                        pool.wait_ge(u_cross, M)
                        fold_first(pool, POOL_SHIFTS, pool_step)
                        pool.wait_ge(pool_step, 1)
                        fold_second(pool, POOL_SHIFTS, pool_step)
                    pool.indirect_dma_start(rows[:, c:c + D], None, table[:, :],
                                            bass.IndirectOffsetOnAxis(ap=idx[:, g:g + 1], axis=0))\
                        .then_inc(gathered[s], 16)

        @block.tensor
        def _(pe):
            pe.wait_ge(ident_ready, 1)
            for n in range(10):
                pe.matmul(bank(TG, 0, 128), ident[:, :], ident[:, :], start=True, stop=True)
            def weights(start, end):
                for x in range(start, end):
                    weight_products(pe, x)

            weights(0, W_ROWS)
            transpose_rows(pe, 0, 0)
            weights(W_ROWS, W_PARTS[0][0])
            transpose_rows(pe, 0, 1)
            pe.wait_ge(fills_ready, 1)
            for s, (x0, x1, x2, x3) in enumerate(W_PARTS):
                t_group(pe, 0, s, 0)
                t_group(pe, 0, s, 1)
                weights(x0, x1)
                t_group(pe, 0, s, 2)
                weights(x1, x2)
                t_group(pe, 0, s, 3)
                weights(x2, x3)
                transpose_rows(pe, (s + 2) // UNITS, (s + 2) % UNITS)
            for v in range(4):
                if v == 2:
                    pe.wait_ge(pool_prod, 1)
                t_group(pe, 0, 3, v)
            pe.wait_ge(u_pairs, M)
            pe.wait_ge(u_cross, M)
            for n in range(V_GROUPS):
                if n == C_BANKS.index(TG):
                    for p in range(2):
                        pe.wait_ge(t_copied[p], UNITS * 4 - 1)
                transpose_coef(pe, n)
                if n == V_GROUPS - 4:
                    transpose_rows(pe, 1, 1)
            n = max(n for n in range(V_GROUPS) if C_BANKS[n % 4] == TG)
            pe.wait_ge(coef_ready[COPIER[n]], COPIER[:n + 1].count(COPIER[n]))
            pe.wait_ge(w0g_in_sb, 16)

            def step(q, s, ahead, last_at):
                for v in range(4):
                    t_group(pe, q, s, v)
                if ahead[2]:
                    transpose_rows(pe, *ahead[2])
                cin(pe, q - 1, last_at, s)

            with pe.Fori(1, CHUNKS - 1) as q:
                t_last = pe.snap((q + 1) % 2 * (COLS * CHUNK))
                chunk(lambda q, s, ahead: step(q, s, ahead, t_last), q)
            c = CHUNKS - 1
            chunk(lambda q, s, ahead: step(q, s, ahead, (c - 1) % 2 * COLS * CHUNK), c, final=True)
            pe.wait_ge(top_in_sb, TOP_DMAS * 16)
            pe.wait_ge(xx_ready, 2 * CHUNKS * UNITS)
            pe.wait_ge(xbd_ready, 2 * CHUNKS * UNITS)
            for p in range(2):
                pe.wait_ge(t_copied[p], CHUNKS * UNITS * 4 - 1)
            for j in range(TOP1 // 128):
                pe.matmul(bank(L1 + j), w1_sb[32 * j:32 * j + DENSE, top1d_at:top1d_at + 128],
                          w1_sb[32 * j:32 * j + DENSE, dense_at:dense_at + B], start=True, stop=False)
            for part in range(4):
                cin(pe, c, c % 2 * COLS * CHUNK, part)
            for n in range(2):
                pe.wait_ge(acc_free, 2 * CHUNKS - 1 + n)
                for j in range(TOP1 // 128):
                    c = top1_at + n * TOP1 + 128 * j
                    last = pe.matmul(bank(L1 + j), w1_sb[:, c:c + 128], w1_sb[:, z_at + n * B:z_at + (n + 1) * B],
                                     start=False, stop=(n == 1))
                    if n == 1:
                        last.then_inc(l1_done, 1)
            for j in range(TOP2 // 128):
                for n in range(TOP1 // 128):
                    if j == 0:
                        pe.wait_ge(l1_ready, n + 1)
                    c = top2_at + n * TOP2 + 128 * j
                    last = pe.matmul(bank(ACC + j), w1_sb[:, c:c + 128],
                                     hid1[n // 2][:, n % 2 * B:(n % 2 + 1) * B], start=(n == 0), stop=(n == 3))
                last.then_inc(l2_done, 1)
            for n in range(TOP2 // 128):
                pe.wait_ge(l2_ready, n + 1)
                for j in range(4):
                    c = n * B + j * B // 4
                    last = pe.matmul(bank(L3, 0, B // 4, 32 * j, 1), top3_sb[:, n:n + 1],
                                     hid2[:, c:c + B // 4], start=(n == 0), stop=(n == 1), tile_position=(0, 32 * j))
            last.then_inc(l3_done, 1)

        @block.scalar
        def _(act):
            def pairs(start, end):
                for x in range(start, end):
                    copy_pairs(act, x)

            act.dma_start(at(t_sb, base_in, [[1, idx.shape[1]]]).bitcast(I32), base).then_inc(ids_in_sb, 16)
            act.dma_start(at(t_sb, cross_in, [[1, 4 * HALF * HALF]]), w0x).then_inc(w0x_in_sb, 16)
            def rows_pieces(q, s):
                return [(f, q, s, g, (k,)) for f in (act_xx, act_xbd) for g in range(2) for k in range(2)]

            def piece(pieces, n):
                for f, q, s, g, ks in pieces[:n]:
                    f(act, q, s, g, ks)
                del pieces[:n]

            pairs(0, W_ROWS)
            pieces = rows_pieces(0, 0)
            piece(pieces, 2)
            for x in range(W_ROWS, W_PARTS[0][0]):
                pairs(x, x + 1)
                if len(pieces) == 4:
                    act.wait_ge(fills_ready, 1)
                piece(pieces, 1)
            for s, (x0, x1, x2, x3) in enumerate(W_PARTS):
                pieces = rows_pieces(0, s + 1)
                piece(pieces, 2)
                act_copy_t(act, 0, 0, s, 0)
                piece(pieces, 1)
                act_copy_t(act, 0, 0, s, 1)
                for x in range(x0, x3):
                    if x == x1:
                        act_copy_t(act, 0, 0, s, 2)
                    if x == x2:
                        act_copy_t(act, 0, 0, s, 3)
                    pairs(x, x + 1)
                    piece(pieces, 1)
            for v in range(4):
                act_copy_t(act, 0, 0, 3, v)
                if v == 0:
                    act.wait_ge(t_copied[1], 3 * 4)
                act_copy_t(act, 0, 0, 3, v, p=1)
                if v == 1:
                    act_xx(act, 1, 0, 0)
            pieces = rows_pieces(1, 0)[2:]
            for n in range(V_GROUPS):
                if COPIER[n] == 0:
                    copy_coef(act, lambda o, i: act.activation(o, i, ACT.Copy), n)
                    piece(pieces, 1)
            for g in range(2):
                act_xx(act, 1, 1, g)

            def step(q, s, ahead, t_at):
                for v in range(4):
                    act_copy_t(act, q, t_at, s, v)
                    if v < 2 and ahead[1]:
                        act_xbd(act, *ahead[1], v)
                if ahead[2]:
                    act_xx(act, *ahead[2], 0)
                    act_xx(act, *ahead[2], 1)
                if s == UNITS - 1:
                    copy_z(act, q - 1)

            act.wait_ge(bias_ready, 1)
            act.wait_ge(u_done, 2 * M)
            with act.Fori(1, CHUNKS - 1) as q:
                t_at = act.snap(q % 2 * (COLS * CHUNK))
                chunk(lambda q, s, ahead: step(q, s, ahead, t_at), q)
            c = CHUNKS - 1
            chunk(lambda q, s, ahead: step(q, s, ahead, c % 2 * COLS * CHUNK), c, final=True)
            copy_z(act, c)
            for j in range(TOP1 // 128):
                act.wait_ge(l1_done, j + 1)
                act.activation(hid1[j // 2][:, j % 2 * B:(j % 2 + 1) * B], bank(L1 + j), ACT.Relu,
                               bias=top_bias[:, j:j + 1]).then_inc(l1_ready, 1)
            for j in range(TOP2 // 128):
                act.wait_ge(l2_done, j + 1)
                act.activation(hid2[:, j * B:(j + 1) * B], bank(ACC + j), ACT.Relu,
                               bias=top_bias[:, 4 + j:5 + j]).then_inc(l2_ready, 1)
            act.wait_ge(l3_done, 1)
            for j in range(2):
                last = act.activation(at(prod[3], 0, [[1, B // 4]], 32 * j, 1), bank(L3, 0, B // 4, 32 * j, 1), ACT.Copy)
            last.then_inc(l3_ready, 1)

        @block.vector
        def _(dve):
            dve.wait_ge(ids_in_sb, 32)
            n = idx.shape[1]
            dve.tensor_tensor(idx[:, :], at(t_sb, ids_in, [[1, n]]).bitcast(I32),
                              at(t_sb, base_in, [[1, n]]).bitcast(I32), ALU.add).then_inc(idx_ready, 1)
            dve.wait_ge(w0p_in_sb, 16)
            n = 4 * VCOLS
            dve.tensor_tensor(w0p_sb[:, :], t_sb[:, pair_in:pair_in + n], t_sb[:, pair_in + n:pair_in + 2 * n],
                              ALU.add).then_inc(w0_ready, 1)
            dve.wait_ge(w0x_in_sb, 16)
            n = HALF * HALF
            dve.tensor_tensor(at(w0x_sb, 0, [[2 * n, 2], [n, 2], [1, n]]), at(t_sb, cross_in, [[n, 2], [0, 2], [1, n]]),
                              at(t_sb, cross_in + 2 * n, [[n, 2], [0, 2], [1, n]]), ALU.add).then_inc(w0_ready, 1)
            def cross_copies(start, end):
                for x in range(start, end):
                    copy_cross(dve, x)

            part = UNIT * 2 * M // 4
            for n in range(8):
                cross_copies(n, n + 1)
                dve.memset(xbd[n // 4][:, n % 4 * part:(n % 4 + 1) * part], 0.0)
                last = dve.memset(at(prod[n // 2], COLS * (1 + SUB * (n % 2)) - 1, [[COLS, SUB]]), 1.0)
            last.then_inc(fills_ready, 1)
            dve.wait_ge(fills_ready, 1)
            cross_copies(8, W_ROWS)
            for n in range(6):
                products(dve, 0, 0, n // 3, n % 3)
                cross_copies(W_ROWS + n, W_ROWS + n + 1)
            for s, (x0, x1, x2, x3) in enumerate(W_PARTS):
                dve_copy_t(dve, 0, 0, s, 0)
                products(dve, 0, s + 1, 0, 0)
                dve_copy_t(dve, 0, 0, s, 1)
                cross_copies(x0, x1)
                products(dve, 0, s + 1, 0, 1)
                dve_copy_t(dve, 0, 0, s, 2)
                cross_copies(x1, x2)
                products(dve, 0, s + 1, 0, 2)
                if x3 < M:
                    products(dve, 0, s + 1, 1, 0)
                dve_copy_t(dve, 0, 0, s, 3)
                if x3 < M:
                    cross_copies(x2, x2 + 1)
                    products(dve, 0, s + 1, 1, 1)
                    cross_copies(x2 + 1, x3)
                    products(dve, 0, s + 1, 1, 2)
                else:
                    cross_copies(x2, x2 + 1)
                    products(dve, 0, s + 1, 1, 2, first=2)
                    cross_copies(x2 + 1, x3)
            dve.wait_ge(u_pairs, M)
            dve.wait_ge(u_cross, M)
            fold_first(dve, DVE_SHIFTS, fold_step)
            dve.wait_ge(fold_step, 1)
            fold_second(dve, (0, SHIFTS), fold_step)
            fold_second(dve, [s for s in DVE_SHIFTS if s % SHIFTS], fold_step)
            copies = [n for n in range(V_GROUPS) if COPIER[n] == 1]
            for n in range(6):
                products(dve, 1, 0, n // 3, n % 3)
                for m in copies[n:n + 1]:
                    copy_coef(dve, dve.tensor_copy, m)
            dve.wait_ge(t_copied[1], UNITS * 4)

            def step(q, s, ahead, t_at):
                for g in range(2):
                    dve_copy_t(dve, q, t_at, s, 2 * g)
                    dve_copy_t(dve, q, t_at, s, 2 * g + 1)
                    if ahead[1]:
                        products(dve, *ahead[1], g)

            dve.wait_ge(small_in_sb, 32)
            dve.tensor_scalar(cin_bias[:, 2:4], cin_bias[:, 0:2], float(D), None, ALU.mult).then_inc(bias_ready, 1)
            with dve.Fori(1, CHUNKS - 1) as q:
                t_at = dve.snap(q % 2 * (COLS * CHUNK))
                chunk(lambda q, s, ahead: step(q, s, ahead, t_at), q)
            c = CHUNKS - 1
            chunk(lambda q, s, ahead: step(q, s, ahead, c % 2 * COLS * CHUNK), c, final=True)

            dve.wait_ge(l3_done, 1)
            for j in range(2, 4):
                last = dve.tensor_copy(at(prod[3], 0, [[1, B // 4]], 32 * j, 1), bank(L3, 0, B // 4, 32 * j, 1))
            last.then_inc(l3_ready, 1)


def _pairs():
    out = np.zeros((2, 2, PAIRS, 2), np.int64)
    for e in range(2):
        for k in range(2):
            at = [(h, (h + s) % HALF) for s in range(SHIFTS * e, SHIFTS * (e + 1)) for h in range(HALF)]
            at += [(h, h + HALF // 2) for h in range(LAST * e, LAST * (e + 1))]
            out[e, k] = np.array(at) + HALF * k
    return out.reshape(4, PAIRS, 2)


def kernel(**inputs):
    import concourse.bacc as bacc
    from concourse import mybir as _mybir
    from concourse.bass_utils import run_bass_kernel_spmd

    a = {name: np.asarray(x) for name, x in inputs.items()}
    tables = [a[f"tbl_{f}"] for f in range(M)]
    starts = np.cumsum([0] + [t.shape[0] for t in tables])[:-1].astype(np.int32)

    ids = a["ids"].reshape(CHUNKS * UNITS, 2, TILES // 2, PER_GATHER, M).transpose(3, 4, 0, 2, 1).reshape(128, -1)
    base = np.ascontiguousarray(np.broadcast_to(np.tile(starts, PER_GATHER)[:, None], ids.shape))

    w0 = a["L0_rec_W0"].reshape(O, M, M)
    w1 = a["L0_rec_W1"].reshape(O, M, O)
    pairs = _pairs()
    w0p = np.zeros((O, 2, 4, VCOLS), w0.dtype)
    w0p[:, 0, :, :PAIRS] = w0[:, pairs[..., 0], pairs[..., 1]]
    other = pairs[..., 0] != pairs[..., 1]
    w0p[:, 1, :, :PAIRS][:, other] = w0[:, pairs[..., 1], pairs[..., 0]][:, other]
    w0p[:, 0, 0, PAIRS] = a["L0_rec_b0"]
    lo, hi = slice(0, HALF), slice(HALF, M)
    w0x = np.stack([w0[:, lo, hi], w0[:, hi, lo], w0[:, hi, lo].transpose(0, 2, 1), w0[:, lo, hi].transpose(0, 2, 1)], axis=1)
    w0g = w0.reshape(O, M, 2, 2, GRAM).transpose(3, 2, 1, 4, 0).reshape(128, GRAM * O)

    arrays = {
        "table": np.concatenate(tables, axis=0),
        "ids": ids,
        "base": base,
        "w1t": w1.transpose(2, 1, 0).reshape(O, M * O),
        "w0p": w0p.reshape(O, -1),
        "w0x": w0x.reshape(O, -1),
        "w0g": w0g,
        "cin_b": np.stack([a["L0_rec_b0"], a["L0_rec_b1"]], axis=1),
        "top1": a["W_top1"][:2 * O].reshape(2, O, TOP1).transpose(1, 0, 2).reshape(O, -1),
        "top1d": a["W_top1"][2 * O:],
        "top2": a["W_top2"].reshape(4, 128, TOP2).transpose(1, 0, 2).reshape(128, -1),
        "top3": a["W_top3"].reshape(2, 128).T,
        "b_top": np.concatenate([a["b_top1"].reshape(4, 128), a["b_top2"].reshape(2, 128)], axis=0).T,
        "dense": a["dense_ctx"].T,
    }
    arrays = {name: np.ascontiguousarray(x) for name, x in arrays.items()}
    nc = bacc.Bacc("TRN2", target_bir_lowering=False, num_devices=1)
    args = [nc.dram_tensor(name, x.shape, _mybir.dt.from_np(x.dtype), kind="ExternalInput").ap()
            for name, x in arrays.items()]
    out = nc.dram_tensor("out", (4, B // 4), _mybir.dt.float32, kind="ExternalOutput").ap()
    build(nc, *args, out)
    r = run_bass_kernel_spmd(nc, [arrays], core_ids=[0])
    return r.results[0]["out"].reshape(B, 1)
```
